# Optimizing a Trainium2 kernel written in Bass

```python
import numpy as np
import jax
import jax.numpy as jnp

def _softmax(x, axis=-1):
    return jax.nn.softmax(x, axis=axis)
def _gelu(x):
    return jax.nn.gelu(x, approximate=True)
def _silu(x):
    return jax.nn.silu(x)
def _sigmoid(x):
    return jax.nn.sigmoid(x)
def _layernorm(x, axis=-1, eps=1e-5):
    m = jnp.mean(x, axis=axis, keepdims=True)
    v = jnp.var(x, axis=axis, keepdims=True)
    return (x - m) / jnp.sqrt(v + eps)
def _scatter_add(tgt, idx, src, axis=0):
    return tgt.at[idx].add(src)
def _segment_sum(src, seg, n):
    return jax.ops.segment_sum(src, seg, n)

kernel_name = 'mk_adj_resnorm_d1_adj_1024_f1cb15'

def setup_inputs(seed: int = 0):
    np.random.seed(seed)
    _w = jnp.asarray
    def _rec_inputs():
        import jax
        import jax.numpy as jnp
        _gk = jax.random.key(seed)
        x = -0.0002928 + 1 * jax.random.normal(jax.random.fold_in(_gk, 1), (32, 512, 1024), jnp.float32)
        _w = (1.0 + jnp.arange(512, dtype=jnp.float32)) ** -0.5
        _w = _w / _w.mean()
        _pij = jnp.clip(0.0625 * _w[:, None] * _w[None, :], 0.0, 1.0)
        _a = jax.random.uniform(jax.random.fold_in(_gk, 2), (32, 512, 512)) < _pij
        adj = _a.astype(jnp.int32)
        return x, adj
    x, adj = _rec_inputs()
    def _L0_gnn_setup():
        import jax, jax.numpy as jnp
        import numpy as np
        NEG_INF = -9000000000000000.0
        ALPHA = 0.2
        H, F = (16, 64)
        key = jax.random.key(seed)
        k1, k2, k3, k4, k5 = jax.random.split(key, 5)
        B, N, D = (8, 512, 1024)
        h = jax.random.normal(k1, (B, N, D), dtype=jnp.float32)
        adj = jax.random.randint(k2, (B, N, N), 0, 2, dtype=jnp.int32)
        adj_weight = jax.random.uniform(k3, (B, N, N), dtype=jnp.float32)
        W = jax.random.normal(k4, (1, D, D), dtype=jnp.float32) * (1.414 * (6.0 / (2 * D)) ** 0.5)
        a = jax.random.normal(k5, (1, H, 2 * F, 1), dtype=jnp.float32) * 0.1
        return {'h': h, 'adj': adj, 'adj_weight': adj_weight, 'W': W, 'a': a}
    _L0_gnn_all = _L0_gnn_setup()
    _L0_gnn_in = {k: v for k, v in _L0_gnn_all.items() if k in ('W', 'a', )}
    del _L0_gnn_all

    return {
        "x": x,
        "adj": adj,
        "L0_gnn_W": _L0_gnn_in["W"],
        "L0_gnn_a": _L0_gnn_in["a"],
    }

def reference(x, adj, L0_gnn_W, L0_gnn_a):
    import jax
    import jax.numpy as jnp
    def _L0_gnn_ref(h, adj, adj_weight, W, a):
        import jax, jax.numpy as jnp
        import numpy as np
        NEG_INF = -9000000000000000.0
        ALPHA = 0.2
        H, F = (16, 64)
        B, N, D = h.shape
        Wh = jnp.matmul(h, W)
        Wh = Wh.reshape(B, N, H, F).transpose(0, 2, 1, 3)
        Wh1 = jnp.matmul(Wh, a[:, :, :F, :])
        Wh2 = jnp.matmul(Wh, a[:, :, F:, :])
        e = jax.nn.leaky_relu(Wh1 + Wh2, negative_slope=ALPHA)
        mask = (adj == 0)[:, None, :, :]
        att = jnp.where(mask, NEG_INF, e)
        att = jax.nn.softmax(att, axis=-1)
        att = att * adj_weight[:, None, :, :]
        h_prime = jnp.matmul(att, Wh)
        h_prime = h_prime.transpose(0, 2, 1, 3).reshape(B, N, H * F)
        return jax.nn.elu(h_prime)

    x = _layernorm(x + _L0_gnn_ref(x, adj, adj, L0_gnn_W, L0_gnn_a), axis=-1)
    return x


_drawn_inputs = setup_inputs


def setup_inputs(seed=0):
    import zlib

    import numpy as np

    out = dict(_drawn_inputs(seed))
    spreads = {}
    factors = {}
    for name, (base, spread) in spreads.items():
        noise = np.random.default_rng([zlib.crc32(name.encode()), seed]).standard_normal(out[name].shape)
        drawn = base * np.exp(spread * noise) if base else spread * noise
        out[name] = jnp.asarray(drawn.astype(out[name].dtype))
    for name, factor in factors.items():
        out[name] = (out[name] * factor).astype(out[name].dtype)
    return out
```

```python
from contextlib import ExitStack

import concourse.bass as bass
from concourse import mybir

P = 128
BANK = 512
ALU = mybir.AluOpType
ACT = mybir.ActivationFunctionType
AX = mybir.AxisListType
F32 = mybir.dt.float32
F32R = mybir.dt.float32r
I32 = mybir.dt.int32

NEG_INF = -9000000000000000.0
ALPHA = 0.2
EPS = 1e-5
BIG = 3.0e38


def gat_layer(nc, x, adj, W, a, out):
    B, N, D = x.shape
    H = a.shape[1]
    F = D // H
    T = N // P
    K = D // P
    HALVES = D // BANK
    HB = BANK // F
    KB = BANK // P
    assert T == 4 and HALVES == 2 and K == 2 * KB and B % 2 == 0 and N == BANK

    x_rows = x.rearrange("b (t p) d -> (b t) p d", p=P)
    adj_rows = adj.rearrange("b (t p) n -> (b t) p n", p=P)
    out_rows = out.rearrange("b (t p) d -> (b t) p d", p=P)
    W_rows = W.rearrange("o (k p) n -> p (o k) n", p=P)
    a_row = a.rearrange("o h f u -> o (h f u)")

    with ExitStack() as ctx:
        def sb(name, shape, dt=F32):
            return ctx.enter_context(nc.sbuf_tensor(name, shape, dt))

        def psum(name, shape):
            return ctx.enter_context(nc.psum_tensor(name, shape, F32))

        def sem(name):
            return ctx.enter_context(nc.semaphore(name))

        W_high = sb("W_high", [P, K, D], F32R)
        W_low = sb("W_low", [P, K, D], F32R)
        x_tile = sb("x_tile", [P, 2, T, D])
        xT_high = sb("xT_high", [P, 2, K, P], F32R)
        xT_low = sb("xT_low", [P, 2, K, P], F32R)
        Wh_high = sb("Wh_high", [P, T, D], F32R)
        Wh_low = sb("Wh_low", [P, T, D], F32R)
        adj_tile = sb("adj_tile", [P, T, N])
        adjT = sb("adjT", [P, T, N], F32R)
        z = sb("z", [P, T, D])
        elu_neg = sb("elu_neg", [P, 2, D])
        Wh_a = sb("Wh_a", [P, D])
        a_sum = sb("a_sum", [P, D])
        ident = sb("ident", [P, P])
        nonzero = sb("nonzero", [P, N], mybir.dt.bfloat16)
        cnt = sb("cnt", [P, 2, T])
        bound = sb("bound", [P, 2, T])
        head_sum = sb("head_sum", [P, T, H])
        e_act = sb("e_act", [P, T, H])
        row_max = sb("row_max", [P, T, H])
        expo = sb("expo", [P, T, 2, H])
        prob = sb("prob", [P, T, 2, H])
        mass = sb("mass", [P, T, 2, H])
        denom = sb("denom", [P, T, H])
        att_scale = sb("att_scale", [P, T, H])
        row_sum = sb("row_sum", [P, T])
        minus_mean = sb("minus_mean", [P, T])
        sq_sum = sb("sq_sum", [P, T])
        var = sb("var", [P, T])
        var_eps = sb("var_eps", [P, T])
        rstd = sb("rstd", [P, T])
        half_power = sb("half_power", [P, 1])
        nodes = sb("nodes", [P, 1])
        inverse_D = sb("inverse_D", [P, 1])
        eps = sb("eps", [P, 1])
        neg_inf = sb("neg_inf", [P, 2])

        xT_ps = [psum(f"xT_ps{c}", [P, KB, P]) for c in range(2)]
        adjT_ps = [psum(f"adjT_ps{c}", [P, T, P]) for c in range(2)]
        Wh_ps = [psum(f"Wh_ps{h}", [P, BANK]) for h in range(2)]
        hp_ps = [psum(f"hp_ps{h}", [P, BANK]) for h in range(2)]

        W_loaded = [sem(f"W_loaded{i}") for i in range(T)]
        a_loaded = sem("a_loaded")
        x_loaded = [[sem(f"x_loaded{q}{t}") for t in range(T)] for q in range(2)]
        adj_loaded = [sem(f"adj_loaded{t}") for t in range(T)]
        out_stored = [sem(f"out_stored{t}") for t in range(T)]
        ident_ready = sem("ident_ready")
        W_high_ready = sem("W_high_ready")
        W_low_ready = sem("W_low_ready")
        const_ready = sem("const_ready")
        a_sum_ready = sem("a_sum_ready")
        adj_float = sem("adj_float")
        xT_done = sem("xT_done")
        adjT_done = sem("adjT_done")
        Wh_done = sem("Wh_done")
        hp_done = sem("hp_done")
        xT_high_ready = sem("xT_high_ready")
        xT_low_ready = sem("xT_low_ready")
        adjT_ready = sem("adjT_ready")
        Wh_high_ready = sem("Wh_high_ready")
        Wh_low_ready = sem("Wh_low_ready")
        Wh_a_ready = sem("Wh_a_ready")
        head_sum_ready = sem("head_sum_ready")
        cnt_ready = sem("cnt_ready")
        bound_raw = sem("bound_raw")
        bound_ready = sem("bound_ready")
        softmax_step = sem("softmax_step")
        prob_ready = sem("prob_ready")
        z_ready = sem("z_ready")
        exp_ready = sem("exp_ready")
        neg_ready = sem("neg_ready")
        residual_ready = sem("residual_ready")
        y_ready = sem("y_ready")
        mean_ready = sem("mean_ready")
        sq_ready = sem("sq_ready")
        var_step = sem("var_step")
        rstd_ready = sem("rstd_ready")
        norm_ready = sem("norm_ready")

        GROUPS = [(0, T - 1), (T - 1, T)]
        SOFTMAX_STEPS = 9

        def over_batches(eng, batch):
            batch(0, 0, 0, True, False)
            with eng.Fori(0, B // 2 - 1) as turn:
                batch(2 * turn + 1, turn, 1, False, False)
                batch(2 * turn + 2, turn + 1, 0, False, False)
            batch(B - 1, B // 2 - 1, 1, False, True)

        block = ctx.enter_context(nc.Block())

        @block.sync
        def _(sp):
            def load_x(n, q, t):
                sp.dma_start(x_tile[:, q, t, :], x_rows[n, :, :]).then_inc(x_loaded[q][t], 16)

            def load_adj(n, t):
                sp.dma_start(adj_tile[:, t, :].bitcast(I32), adj_rows[n, :, :]).then_inc(adj_loaded[t], 16)

            def store(n, t):
                sp.wait_ge(norm_ready, n + 1)
                sp.dma_start(out_rows[n, :, :], z[:, t, :]).then_inc(out_stored[t], 16)

            load_x(0, 0, 0)
            for k in range(T):
                sp.dma_start(z[:, k, :], W_rows[:, k, :]).then_inc(W_loaded[k], 16)
            load_adj(0, 0)
            for k in range(T, K):
                sp.wait_ge(W_low_ready, k - T + 1)
                sp.dma_start(z[:, k - T, :], W_rows[:, k, :]).then_inc(W_loaded[k - T], 16)
                if k == T:
                    load_x(1, 0, 1)
            for t in range(1, T):
                load_adj(t, t)
                if t > 1:
                    load_x(t, 0, t)

            def batch(b, visit, q, first, last):
                for t in range(T):
                    n = T * b + t
                    if not last:
                        if not first:
                            sp.wait_ge(residual_ready, n - T + 1)
                        load_x(n + T, 1 - q, t)
                        sp.wait_ge(adjT_done, n + 1)
                        sp.wait_ge(cnt_ready, n + 1)
                        load_adj(n + T, t)
                    if not first and t > 0:
                        store(n - T - 1, t - 1)
                if not first:
                    store(T * b - 1, T - 1)

            over_batches(sp, batch)
            for t in range(T):
                store(T * (B - 1) + t, t)
            for t in range(T):
                sp.wait_ge(out_stored[t], 16 * B)

        @block.tensor
        def _(pe):
            def transpose_x(n, visit, q, t, first):
                pe.wait_ge(x_loaded[q][t], 16 * (visit + 1))
                for c in range(2):
                    if not first:
                        pe.wait_ge(xT_low_ready, 2 * n + c - 1)
                    for k in range(KB):
                        block_k = x_tile[:, q, t, (c * KB + k) * P:(c * KB + k + 1) * P]
                        done = nc.tensor.transpose(xT_ps[c][:, k, :], block_k, ident[:])
                    done.then_inc(xT_done, 1)

            def transpose_adj(n, t, wait_bank):
                pe.wait_ge(adj_float, n + 1)
                if wait_bank:
                    pe.wait_ge(adjT_ready, n - 1)
                for j in range(T):
                    done = nc.tensor.transpose(adjT_ps[t % 2][:, j, :], adj_tile[:, t, j * P:(j + 1) * P],
                                               ident[:])
                done.then_inc(adjT_done, 1)

            pe.wait_ge(ident_ready, 2)
            transpose_x(0, 0, 0, 0, True)

            def batch(b, visit, q, first, last):
                for t in range(T):
                    n = T * b + t
                    if t < T - 1:
                        transpose_x(n + 1, visit, q, t + 1, False)
                    elif not last:
                        transpose_x(n + 1, visit + q, 1 - q, 0, False)
                    transpose_adj(n, t, not first or t >= 2)
                    for h in range(HALVES):
                        cols = slice(h * BANK, (h + 1) * BANK)
                        if not first or t > 0:
                            pe.wait_ge(Wh_a_ready, 2 * n + h - 1)
                        for k in range(K):
                            if h == 0 and k % KB == 0:
                                pe.wait_ge(xT_low_ready, 2 * n + k // KB + 1)
                            if first and t == 0 and h == 0:
                                pe.wait_ge(W_low_ready, k + 1)
                            high, low = xT_high[:, t % 2, k, :], xT_low[:, t % 2, k, :]
                            nc.tensor.matmul(Wh_ps[h][:], high, W_high[:, k, cols], start=(k == 0), stop=False)
                            nc.tensor.matmul(Wh_ps[h][:], high, W_low[:, k, cols], start=False, stop=False)
                            done = nc.tensor.matmul(Wh_ps[h][:], low, W_high[:, k, cols],
                                                    start=False, stop=(k == K - 1))
                        done.then_inc(Wh_done, 1)
                pe.wait_ge(adjT_ready, T * b + T)
                for t in range(T):
                    for h in range(HALVES):
                        cols = slice(h * BANK, (h + 1) * BANK)
                        g = 2 * (T * b + t) + h
                        if not first or t > 0:
                            pe.wait_ge(z_ready, g - 1)
                        for j in range(T):
                            if t == 0:
                                pe.wait_ge(Wh_low_ready, 2 * (T * b + j) + h + 1)
                            weights = adjT[:, j, t * P:(t + 1) * P]
                            nc.tensor.matmul(hp_ps[h][:], weights, Wh_high[:, j, cols],
                                             start=(j == 0), stop=False)
                            done = nc.tensor.matmul(hp_ps[h][:], weights, Wh_low[:, j, cols],
                                                    start=False, stop=(j == T - 1))
                        done.then_inc(hp_done, 1)

            over_batches(pe, batch)

        @block.scalar
        def _(act):
            def split_x(n, t, ):
                for c in range(2):
                    act.wait_ge(xT_done, 2 * n + c + 1)
                    nc.scalar.activation(xT_high[:, t % 2, c * KB:(c + 1) * KB, :], xT_ps[c][:],
                                         ACT.Copy).then_inc(xT_high_ready, 1)

            def exp_z(m, t, wait_square):
                act.wait_ge(z_ready, 2 * m + 2)
                if wait_square:
                    act.wait_ge(sq_ready, m - 1)
                nc.scalar.activation(elu_neg[:, t % 2, :], z[:, t, :], ACT.Exp).then_inc(exp_ready, 1)

            def square(m, t):
                act.wait_ge(mean_ready, m + 1)
                nc.scalar.activation(elu_neg[:, t % 2, :], z[:, t, :], ACT.Square,
                                     bias=minus_mean[:, t:t + 1],
                                     accum_out=sq_sum[:, t:t + 1]).then_inc(sq_ready, 1)

            def softmax_exp(b, g):
                lo, hi = GROUPS[g]
                act.wait_ge(softmax_step, SOFTMAX_STEPS * (2 * b + g) + 5)
                nc.scalar.activation(prob[:, lo:hi, :, :], expo[:, lo:hi, :, :], ACT.Exp).then_inc(prob_ready, 1)

            for k in range(K):
                act.wait_ge(W_loaded[k % T], 16 * (k // T + 1))
                nc.scalar.activation(W_high[:, k, :], z[:, k % T, :], ACT.Copy).then_inc(W_high_ready, 1)
                if k == 0:
                    split_x(0, 0)

            def batch(b, visit, q, first, last):
                for t in range(T):
                    n = T * b + t
                    if not first:
                        exp_z(n - T, t, t >= 2)
                    if t < T - 1 or not last:
                        split_x(n + 1, t + 1)
                    act.wait_ge(adjT_done, n + 1)
                    nc.scalar.activation(adjT[:, :, t * P:(t + 1) * P], adjT_ps[t % 2][:],
                                         ACT.Copy).then_inc(adjT_ready, 1)
                    if t == T - 1:
                        softmax_exp(b, 0)
                    for h in range(HALVES):
                        act.wait_ge(Wh_done, 2 * n + h + 1)
                        nc.scalar.activation(Wh_high[:, t, h * BANK:(h + 1) * BANK], Wh_ps[h][:],
                                             ACT.Copy).then_inc(Wh_high_ready, 1)
                        if h == 0 and not first:
                            square(n - T, t)
                softmax_exp(b, 1)
                if not first:
                    act.wait_ge(sq_ready, T * b)

            over_batches(act, batch)
            for t in range(T):
                m = T * (B - 1) + t
                exp_z(m, t, t >= 2)
                square(m, t)

        @block.vector
        def _(dve):
            def split_x(n, t):
                for c in range(2):
                    chunks = slice(c * KB, (c + 1) * KB)
                    dve.wait_ge(xT_high_ready, 2 * n + c + 1)
                    nc.vector.tensor_tensor(xT_low[:, t % 2, chunks, :], xT_ps[c][:],
                                            xT_high[:, t % 2, chunks, :].bitcast(F32),
                                            ALU.subtract).then_inc(xT_low_ready, 1)

            def clip_exp(m, t):
                dve.wait_ge(exp_ready, m + 1)
                nc.vector.tensor_scalar(elu_neg[:, t % 2, :], elu_neg[:, t % 2, :], 1.0, -1.0,
                                        ALU.min, ALU.add).then_inc(neg_ready, 1)

            def residual_sum(m, t):
                dve.wait_ge(residual_ready, m + 1)
                nc.vector.scalar_tensor_tensor(z[:, t, :], z[:, t, :], 0.0, elu_neg[:, t % 2, :],
                                               ALU.max, ALU.add,
                                               accum_out=row_sum[:, t:t + 1]).then_inc(y_ready, 1)
                dve.wait_ge(y_ready, m + 1)
                nc.vector.tensor_scalar(minus_mean[:, t:t + 1], row_sum[:, t:t + 1], -1.0 / D, None,
                                        ALU.mult).then_inc(mean_ready, 1)

            def normalise(m, t):
                dve.wait_ge(rstd_ready, m + 1)
                nc.vector.tensor_scalar(z[:, t, :], z[:, t, :], minus_mean[:, t:t + 1], rstd[:, t:t + 1],
                                        ALU.add, ALU.mult).then_inc(norm_ready, 1)

            def split_Wh(n, t, h, start):
                cols = slice(h * BANK, (h + 1) * BANK)
                dve.wait_ge(Wh_high_ready, 2 * n + h + 1)
                nc.vector.tensor_tensor(Wh_low[:, t, cols], Wh_ps[h][:], Wh_high[:, t, cols].bitcast(F32),
                                        ALU.subtract).then_inc(Wh_low_ready, 1)
                if h == 0 and not start:
                    dve.wait_ge(head_sum_ready, n)
                nc.vector.tensor_tensor(Wh_a[:, cols], Wh_ps[h][:], a_sum[:, cols],
                                        ALU.mult).then_inc(Wh_a_ready, 1)

            def sum_heads(n, t):
                dve.wait_ge(Wh_a_ready, 2 * n + 2)
                nc.vector.tensor_reduce(head_sum[:, t, :], Wh_a[:].rearrange("p (h f) -> p h f", f=F),
                                        AX.X, ALU.add).then_inc(head_sum_ready, 1)

            def step(done, b, g, i):
                done.then_inc(softmax_step, 1)
                dve.wait_ge(softmax_step, SOFTMAX_STEPS * (2 * b + g) + i)

            def exponents(b, g, first):
                lo, hi = GROUPS[g]
                shape = [P, hi - lo, H]
                s, e, m = head_sum[:, lo:hi, :], e_act[:, lo:hi, :], row_max[:, lo:hi, :]
                dve.wait_ge(head_sum_ready, T * b + hi)
                if not first or g > 0:
                    dve.wait_ge(softmax_step, SOFTMAX_STEPS * (2 * b + g))
                dve.wait_ge(bound_ready, T * b + hi)
                step(nc.vector.scalar_tensor_tensor(e, s, ALPHA, s, ALU.mult, ALU.max), b, g, 1)
                step(nc.vector.tensor_tensor(m, e, bound[:, 0, lo:hi].unsqueeze(2).to_broadcast(shape), ALU.max),
                     b, g, 2)
                step(nc.vector.tensor_tensor(m, m, bound[:, 1, lo:hi].unsqueeze(2).to_broadcast(shape), ALU.min),
                     b, g, 3)
                nc.vector.tensor_scalar(expo[:, lo:hi, 1, :], m, -1.0, NEG_INF, ALU.mult, ALU.add)
                step(nc.vector.tensor_tensor(expo[:, lo:hi, 0, :], e, m, ALU.subtract), b, g, 4)
                nc.vector.tensor_scalar(expo[:, lo:hi, :, :], expo[:, lo:hi, :, :], 0.0, None,
                                        ALU.min).then_inc(softmax_step, 1)

            def scales(b, g, first):
                lo, hi = GROUPS[g]
                shape = [P, hi - lo, H]
                dve.wait_ge(prob_ready, 2 * b + g + 1)
                nc.vector.tensor_tensor(mass[:, lo:hi, 0, :], prob[:, lo:hi, 0, :],
                                        cnt[:, 0, lo:hi].unsqueeze(2).to_broadcast(shape), ALU.mult)
                step(nc.vector.tensor_tensor(mass[:, lo:hi, 1, :], prob[:, lo:hi, 1, :],
                                             cnt[:, 1, lo:hi].unsqueeze(2).to_broadcast(shape), ALU.mult),
                     b, g, 6)
                step(nc.vector.tensor_tensor(denom[:, lo:hi, :], mass[:, lo:hi, 0, :], mass[:, lo:hi, 1, :],
                                             ALU.add), b, g, 7)
                step(nc.vector.reciprocal(denom[:, lo:hi, :], denom[:, lo:hi, :]), b, g, 8)
                if not first:
                    dve.wait_ge(z_ready, 2 * T * b)
                step(nc.vector.tensor_tensor(att_scale[:, lo:hi, :], prob[:, lo:hi, 0, :], denom[:, lo:hi, :],
                                             ALU.mult), b, g, 9)

            def scale_rows(b, t, h, first):
                n = T * b + t
                dve.wait_ge(softmax_step, SOFTMAX_STEPS * (2 * b + (1 if t == T - 1 else 0) + 1))
                dve.wait_ge(hp_done, 2 * n + h + 1)
                if not first and h == 0:
                    dve.wait_ge(out_stored[t], 16 * b)
                nc.vector.tensor_tensor(
                    z[:, t, h * BANK:(h + 1) * BANK].rearrange("p (a f) -> p a f", f=F),
                    hp_ps[h][:].rearrange("p (a f) -> p a f", f=F),
                    att_scale[:, t, h * HB:(h + 1) * HB].unsqueeze(2).to_broadcast([P, HB, F]),
                    ALU.mult).then_inc(z_ready, 1)

            def adj_to_float(b, t):
                dve.wait_ge(adj_loaded[t], 16 * (b + 1))
                nc.vector.tensor_copy(adj_tile[:, t, :], adj_tile[:, t, :].bitcast(I32)).then_inc(adj_float, 1)

            for k in range(K):
                dve.wait_ge(W_high_ready, k + 1)
                nc.vector.tensor_tensor(W_low[:, k, :], z[:, k % T, :], W_high[:, k, :].bitcast(F32),
                                        ALU.subtract).then_inc(W_low_ready, 1)
                if k == 0:
                    split_x(0, 0)
            dve.wait_ge(a_loaded, 16)
            a_parts = elu_neg[:].rearrange("p q (h s f) -> p (q h) s f", s=2, f=F)
            nc.vector.tensor_tensor(a_sum[:].rearrange("p (h f) -> p h f", f=F), a_parts[:, :, 0, :],
                                    a_parts[:, :, 1, :], ALU.add).then_inc(a_sum_ready, 1)
            dve.wait_ge(a_sum_ready, 1)
            adj_to_float(0, 0)

            def batch(b, visit, q, first, last):
                for t in range(T):
                    n = T * b + t
                    if not first:
                        clip_exp(n - T, t)
                    if t < T - 1 or not last:
                        split_x(n + 1, t + 1)
                    if t < T - 1:
                        adj_to_float(b, t + 1)
                    elif not last:
                        adj_to_float(b + 1, 0)
                    dve.wait_ge(adj_float, n + 1)
                    if not first or t > 0:
                        dve.wait_ge(cnt_ready, n)
                    nc.vector.tensor_scalar(nonzero[:], adj_tile[:, t, :], 0.0, None, ALU.not_equal, ALU.add,
                                            accum_out=cnt[:, 0, t:t + 1]).then_inc(cnt_ready, 1)
                    if not first and t > 0:
                        normalise(n - T - 1, t - 1)
                    if t == T - 1:
                        exponents(b, 0, first)
                    split_Wh(n, t, 0, first and t == 0)
                    if t == T - 1:
                        scales(b, 0, first)
                    if not first:
                        residual_sum(n - T, t)
                    split_Wh(n, t, 1, first and t == 0)
                    if t < T - 1:
                        sum_heads(n, t)
                scale_rows(b, 0, 0, first)
                scale_rows(b, 0, 1, first)
                sum_heads(T * b + T - 1, T - 1)
                scale_rows(b, 1, 0, first)
                exponents(b, 1, first)
                scale_rows(b, 1, 1, first)
                scale_rows(b, 2, 0, first)
                scales(b, 1, first)
                scale_rows(b, 2, 1, first)
                if not first:
                    normalise(T * b - 1, T - 1)
                if last:
                    clip_exp(T * b, 0)
                    residual_sum(T * b, 0)
                scale_rows(b, 3, 0, first)
                scale_rows(b, 3, 1, first)

            over_batches(dve, batch)
            for t in range(1, T):
                m = T * (B - 1) + t
                clip_exp(m, t)
                residual_sum(m, t)
                normalise(m - 1, t - 1)
            normalise(T * B - 1, T - 1)

        @block.gpsimd
        def _(pool):
            pool.memset(ident[:], 0.0).then_inc(ident_ready, 1)
            pool.wait_ge(ident_ready, 1)
            pool.affine_select(out=ident[:], in_=ident[:], compare_op=ALU.not_equal, fill=1.0, base=0,
                               pattern=[[-1, P]], channel_multiplier=1).then_inc(ident_ready, 1)
            for const, value in ((half_power, -0.5), (nodes, float(N)), (inverse_D, 1.0 / D), (eps, EPS),
                                 (neg_inf, NEG_INF)):
                pool.memset(const[:], value).then_inc(const_ready, 1)
            pool.dma_start(elu_neg[:].rearrange("p q d -> p (q d)"),
                           a_row.to_broadcast([P, 2 * D])).then_inc(a_loaded, 16)
            pool.wait_ge(const_ready, 5)

            def row_bounds(n, t, start):
                pool.wait_ge(cnt_ready, n + 1)
                if not start:
                    pool.wait_ge(bound_ready, n)
                c = cnt[:, 0, t:t + 1]
                pool.tensor_tensor(cnt[:, 1, t:t + 1], nodes[:], c, ALU.subtract)
                pool.tensor_scalar(bound[:, 0, t:t + 1], c, float(N), -BIG, ALU.is_ge, ALU.mult)\
                    .then_inc(bound_raw, 1)
                pool.tensor_scalar(bound[:, 1, t:t + 1], c, 0.0, BIG, ALU.is_gt, ALU.mult).then_inc(bound_raw, 1)
                pool.wait_ge(bound_raw, 2 * n + 2)
                pool.tensor_tensor(bound[:, :, t:t + 1], bound[:, :, t:t + 1], neg_inf[:].unsqueeze(2), ALU.add)\
                    .then_inc(bound_ready, 1)

            def add_x(m, q, t):
                pool.wait_ge(neg_ready, m + 1)
                pool.tensor_tensor(elu_neg[:, t % 2, :], elu_neg[:, t % 2, :], x_tile[:, q, t, :],
                                   ALU.add).then_inc(residual_ready, 1)

            def inverse_std(m, t):
                pool.wait_ge(sq_ready, m + 1)
                pool.tensor_tensor(var[:, t:t + 1], sq_sum[:, t:t + 1], inverse_D[:], ALU.mult)\
                    .then_inc(var_step, 1)
                pool.wait_ge(var_step, 2 * m + 1)
                pool.tensor_tensor(var_eps[:, t:t + 1], var[:, t:t + 1], eps[:], ALU.add).then_inc(var_step, 1)
                pool.wait_ge(var_step, 2 * m + 2)
                pool.tensor_tensor(rstd[:, t:t + 1], var_eps[:, t:t + 1], half_power[:],
                                   ALU.pow).then_inc(rstd_ready, 1)


            def batch(b, visit, q, first, last):
                for t in range(T):
                    n = T * b + t
                    row_bounds(n, t, first and t == 0)
                    if not first:
                        add_x(n - T, 1 - q, t)
                        inverse_std(n - T, t)

            over_batches(pool, batch)
            for t in range(T):
                m = T * (B - 1) + t
                add_x(m, 1, t)
                inverse_std(m, t)


def kernel(x, adj, L0_gnn_W, L0_gnn_a):
    import numpy as np
    import concourse.bacc as bacc
    from concourse.bass_utils import run_bass_kernel_spmd

    nc = bacc.Bacc("TRN2", target_bir_lowering=False, num_devices=1)
    arrays, args = {}, []
    for name, value in (("x", x), ("adj", adj), ("W", L0_gnn_W), ("a", L0_gnn_a)):
        arrays[f"in_{name}"] = np.ascontiguousarray(value)
        args.append(nc.dram_tensor(f"in_{name}", arrays[f"in_{name}"].shape,
                                   mybir.dt.from_np(arrays[f"in_{name}"].dtype), kind="ExternalInput").ap())
    out = nc.dram_tensor("out", arrays["in_x"].shape, F32, kind="ExternalOutput").ap()
    gat_layer(nc, *args, out)
    result = run_bass_kernel_spmd(nc, [arrays], core_ids=[0])
    return result.results[0]["out"]
```

```python
from contextlib import ExitStack

import concourse.bass as bass
from concourse import mybir

P = 128
BANK = 512
ALU = mybir.AluOpType
ACT = mybir.ActivationFunctionType
AX = mybir.AxisListType
F32 = mybir.dt.float32
F32R = mybir.dt.float32r
I32 = mybir.dt.int32

NEG_INF = -9000000000000000.0
ALPHA = 0.2
EPS = 1e-5
WIDE = 4096.0
BIG = 3.0e38


def gat_layer(nc, x, adj, W, a, out):
    B, N, D = x.shape
    H = a.shape[1]
    F = D // H
    T = N // P
    K = D // P
    HALVES = D // BANK
    HB = BANK // F
    KB = BANK // P
    assert T == 4 and HALVES == 2 and K == 2 * KB and B % 2 == 0 and N == BANK

    x_rows = x.rearrange("b (t p) d -> (b t) p d", p=P)
    adj_rows = adj.rearrange("b (t p) n -> (b t) p n", p=P)
    out_rows = out.rearrange("b (t p) d -> (b t) p d", p=P)
    W_rows = W.rearrange("o (k p) n -> p (o k) n", p=P)
    a_row = a.rearrange("o h f u -> o (h f u)")

    with ExitStack() as ctx:
        def sb(name, shape, dt=F32):
            return ctx.enter_context(nc.sbuf_tensor(name, shape, dt))

        def psum(name, shape):
            return ctx.enter_context(nc.psum_tensor(name, shape, F32))

        def sem(name):
            return ctx.enter_context(nc.semaphore(name))

        W_high = sb("W_high", [P, K, D], F32R)
        W_low = sb("W_low", [P, K, D], F32R)
        x_tile = sb("x_tile", [P, 2, T, D])
        xT_high = sb("xT_high", [P, 2, K, P], F32R)
        xT_low = sb("xT_low", [P, 2, K, P], F32R)
        Wh_high = sb("Wh_high", [P, T, D], F32R)
        Wh_low = sb("Wh_low", [P, T, D], F32R)
        adj_tile = sb("adj_tile", [P, T, N])
        adjT = sb("adjT", [P, T, N], F32R)
        adjT_low = sb("adjT_low", [P, T, N], F32R)
        adj_sq = sb("adj_sq", [P, N], mybir.dt.bfloat16)
        adj_sq_sum = sb("adj_sq_sum", [P, T])
        wide_row = sb("wide_row", [P, T])
        wide_rows = sb("wide_rows", [P, 1])
        wide_count = sb("wide_count", [1, 1], I32)
        ones = sb("ones", [P, 1])
        z = sb("z", [P, T, D])
        elu_neg = sb("elu_neg", [P, 2, D])
        Wh_a = sb("Wh_a", [P, D])
        a_sum = sb("a_sum", [P, D])
        ident = sb("ident", [P, P])
        nonzero = sb("nonzero", [P, N], mybir.dt.bfloat16)
        cnt = sb("cnt", [P, 2, T])
        bound = sb("bound", [P, 2, T])
        head_sum = sb("head_sum", [P, T, H])
        e_act = sb("e_act", [P, T, H])
        row_max = sb("row_max", [P, T, H])
        expo = sb("expo", [P, T, 2, H])
        prob = sb("prob", [P, T, 2, H])
        mass = sb("mass", [P, T, 2, H])
        denom = sb("denom", [P, T, H])
        att_scale = sb("att_scale", [P, T, H])
        row_sum = sb("row_sum", [P, T])
        minus_mean = sb("minus_mean", [P, T])
        sq_sum = sb("sq_sum", [P, T])
        var = sb("var", [P, T])
        var_eps = sb("var_eps", [P, T])
        rstd = sb("rstd", [P, T])
        shift = sb("shift", [P, T])
        half_power = sb("half_power", [P, 1])
        nodes = sb("nodes", [P, 1])
        inverse_D = sb("inverse_D", [P, 1])
        eps = sb("eps", [P, 1])
        neg_inf = sb("neg_inf", [P, 2])

        exp_place = [elu_neg[:, t % 2, :] for t in range(T)]
        exp_place_last = [elu_neg[:, 0, :], elu_neg[:, 1, :], Wh_a[:], a_sum[:]]

        xT_ps = [psum(f"xT_ps{c}", [P, KB, P]) for c in range(2)]
        adjT_ps = [psum(f"adjT_ps{c}", [P, T, P]) for c in range(2)]
        Wh_ps = [psum(f"Wh_ps{h}", [P, BANK]) for h in range(2)]
        hp_ps = [psum(f"hp_ps{h}", [P, BANK]) for h in range(2)]

        W_loaded = [sem(f"W_loaded{i}") for i in range(T)]
        a_loaded = sem("a_loaded")
        x_loaded = [[sem(f"x_loaded{q}{t}") for t in range(T)] for q in range(2)]
        adj_loaded = [sem(f"adj_loaded{t}") for t in range(T)]
        out_stored = [sem(f"out_stored{t}") for t in range(T)]
        ident_ready = sem("ident_ready")
        W_high_ready = sem("W_high_ready")
        W_low_ready = sem("W_low_ready")
        const_ready = sem("const_ready")
        a_sum_ready = sem("a_sum_ready")
        adj_float = sem("adj_float")
        xT_done = sem("xT_done")
        adjT_done = sem("adjT_done")
        Wh_done = sem("Wh_done")
        hp_done = sem("hp_done")
        xT_high_ready = sem("xT_high_ready")
        xT_low_ready = sem("xT_low_ready")
        adjT_ready = sem("adjT_ready")
        adjT_low_ready = sem("adjT_low_ready")
        adj_sq_ready = sem("adj_sq_ready")
        wide_ready = sem("wide_ready")
        wide_summed = sem("wide_summed")
        wide_count_ready = sem("wide_count_ready")
        Wh_high_ready = sem("Wh_high_ready")
        Wh_low_ready = sem("Wh_low_ready")
        Wh_a_ready = sem("Wh_a_ready")
        head_sum_ready = sem("head_sum_ready")
        cnt_ready = sem("cnt_ready")
        bound_raw = sem("bound_raw")
        bound_ready = sem("bound_ready")
        softmax_step = sem("softmax_step")
        prob_ready = sem("prob_ready")
        z_ready = sem("z_ready")
        exp_ready = sem("exp_ready")
        below_ready = sem("below_ready")
        residual_ready = sem("residual_ready")
        y_ready = sem("y_ready")
        mean_ready = sem("mean_ready")
        sq_ready = sem("sq_ready")
        var_step = sem("var_step")
        power_ready = sem("power_ready")
        rstd_ready = sem("rstd_ready")
        norm_ready = sem("norm_ready")

        GROUPS = [(0, T - 1), (T - 1, T)]
        SOFTMAX_STEPS = 9

        def over_batches(eng, batch):
            batch(0, 0, 0, True, False)
            with eng.Fori(0, B // 2 - 1) as turn:
                batch(2 * turn + 1, turn, 1, False, False)
                batch(2 * turn + 2, turn + 1, 0, False, False)
            batch(B - 1, B // 2 - 1, 1, False, True)

        block = ctx.enter_context(nc.Block())

        @block.sync
        def _(sp):
            def load_x(n, q, t):
                sp.dma_start(x_tile[:, q, t, :], x_rows[n, :, :]).then_inc(x_loaded[q][t], 16)

            def load_adj(n, t):
                sp.dma_start(adj_tile[:, t, :].bitcast(I32), adj_rows[n, :, :]).then_inc(adj_loaded[t], 16)

            def store(n, t):
                sp.wait_ge(norm_ready, n + 1)
                sp.dma_start(out_rows[n, :, :], z[:, t, :]).then_inc(out_stored[t], 16)

            load_x(0, 0, 0)
            for k in range(T):
                sp.dma_start(z[:, k, :], W_rows[:, k, :]).then_inc(W_loaded[k], 16)
            for k in range(T, K):
                sp.wait_ge(W_low_ready, k - T + 1)
                sp.dma_start(z[:, k - T, :], W_rows[:, k, :]).then_inc(W_loaded[k - T], 16)
            load_adj(0, 0)
            load_x(1, 0, 1)
            sp.dma_start(elu_neg[:].rearrange("p q d -> p (q d)"),
                         a_row.to_broadcast([P, 2 * D])).then_inc(a_loaded, 16)
            for t in range(1, T):
                load_adj(t, t)
                if t > 1:
                    load_x(t, 0, t)

            def batch(b, visit, q, first, last):
                for t in range(T):
                    n = T * b + t
                    if not last:
                        if not first:
                            sp.wait_ge(residual_ready, n - T + 1)
                        load_x(n + T, 1 - q, t)
                        sp.wait_ge(adjT_done, n + 1)
                        sp.wait_ge(cnt_ready, n + 1)
                        sp.wait_ge(adj_sq_ready, n + 1)
                        load_adj(n + T, t)
                    if not first and t > 0:
                        store(n - T - 1, t - 1)
                if not first:
                    store(T * b - 1, T - 1)

            over_batches(sp, batch)
            for t in range(T):
                store(T * (B - 1) + t, t)
            for t in range(T):
                sp.wait_ge(out_stored[t], 16 * B)

        @block.tensor
        def _(pe):
            def transpose_x(n, visit, q, t, first):
                pe.wait_ge(x_loaded[q][t], 16 * (visit + 1))
                for c in range(2):
                    if not first:
                        pe.wait_ge(xT_low_ready, 2 * n + c - 1)
                    for k in range(KB):
                        block_k = x_tile[:, q, t, (c * KB + k) * P:(c * KB + k + 1) * P]
                        done = nc.tensor.transpose(xT_ps[c][:, k, :], block_k, ident[:])
                    done.then_inc(xT_done, 1)

            def transpose_adj(n, t, wait_bank):
                pe.wait_ge(adj_float, n + 1)
                if wait_bank:
                    pe.wait_ge(adjT_low_ready, n - 1)
                for j in range(T):
                    done = nc.tensor.transpose(adjT_ps[t % 2][:, j, :], adj_tile[:, t, j * P:(j + 1) * P],
                                               ident[:])
                done.then_inc(adjT_done, 1)

            def product(t, k, h):
                high, low = xT_high[:, t % 2, k, :], xT_low[:, t % 2, k, :]
                cols = slice(h * BANK, (h + 1) * BANK)
                nc.tensor.matmul(Wh_ps[h][:], high, W_high[:, k, cols], start=(k == 0), stop=False)
                nc.tensor.matmul(Wh_ps[h][:], high, W_low[:, k, cols], start=False, stop=False)
                return nc.tensor.matmul(Wh_ps[h][:], low, W_high[:, k, cols], start=False, stop=(k == K - 1))

            def aggregate(b, first, adj_parts):
                pe.wait_ge(adjT_low_ready, T * b + T)
                for t in range(T):
                    for h in range(HALVES):
                        cols = slice(h * BANK, (h + 1) * BANK)
                        g = 2 * (T * b + t) + h
                        if not first or t > 0:
                            pe.wait_ge(z_ready, g - 1)
                        for j in range(T):
                            if t == 0:
                                pe.wait_ge(Wh_low_ready, 2 * (T * b + j) + h + 1)
                            for part in adj_parts:
                                weights = part[:, j, t * P:(t + 1) * P]
                                nc.tensor.matmul(hp_ps[h][:], weights, Wh_high[:, j, cols],
                                                 start=(j == 0 and part is adjT), stop=False)
                                done = nc.tensor.matmul(hp_ps[h][:], weights, Wh_low[:, j, cols], start=False,
                                                        stop=(j == T - 1 and part is adj_parts[-1]))
                        done.then_inc(hp_done, 1)

            def first_product():
                for k in range(K):
                    if k == K - 1:
                        transpose_x(1, 0, 0, 1, False)
                        transpose_adj(0, 0, False)
                    if k % KB == 0:
                        pe.wait_ge(xT_low_ready, k // KB + 1)
                    pe.wait_ge(W_low_ready, k + 1)
                    for h in range(HALVES):
                        done = product(0, k, h)
                        if k == K - 1:
                            done.then_inc(Wh_done, 1)

            pe.wait_ge(ident_ready, 2)
            pe.wait_ge(const_ready, 6)
            transpose_x(0, 0, 0, 0, True)

            def batch(b, visit, q, first, last):
                for t in range(T):
                    n = T * b + t
                    if first and t == 0:
                        first_product()
                        continue
                    if t < T - 1:
                        transpose_x(n + 1, visit, q, t + 1, False)
                    elif not last:
                        transpose_x(n + 1, visit + q, 1 - q, 0, False)
                    transpose_adj(n, t, not first or t >= 2)
                    for h in range(HALVES):
                        pe.wait_ge(Wh_a_ready, 2 * n + h - 1)
                        for k in range(K):
                            if h == 0 and k % KB == 0:
                                pe.wait_ge(xT_low_ready, 2 * n + k // KB + 1)
                            if t == T - 1 and h == 1 and k == 2:
                                pe.wait_ge(wide_ready, b + 1)
                                nc.tensor.matmul(adjT_ps[0][0:1, 0, 0:1], wide_rows[:], ones[:],
                                                 start=True, stop=True).then_inc(wide_summed, 1)
                            if t == T - 1 and h == 1 and k == K - 1:
                                pe.wait_ge(wide_count_ready, b + 1)
                            done = product(t, k, h)
                        done.then_inc(Wh_done, 1)
                wide = pe.value_load(wide_count[0:1, 0:1], min_val=0, max_val=N)
                with pe.If(wide > 0):
                    aggregate(b, first, (adjT, adjT_low))
                with pe.Else():
                    aggregate(b, first, (adjT,))

            over_batches(pe, batch)

        @block.scalar
        def _(act):
            def split_x(n, t):
                for c in range(2):
                    act.wait_ge(xT_done, 2 * n + c + 1)
                    nc.scalar.activation(xT_high[:, t % 2, c * KB:(c + 1) * KB, :], xT_ps[c][:],
                                         ACT.Copy).then_inc(xT_high_ready, 1)

            def below_zero(m, t, place=exp_place):
                act.wait_ge(z_ready, 2 * m + 2)
                nc.scalar.activation(place[t], z[:, t, :], ACT.Relu, scale=-1.0).then_inc(below_ready, 1)

            def exp_z(m, t, place=exp_place):
                act.wait_ge(below_ready, m + 1)
                nc.scalar.activation(place[t], place[t], ACT.Exp, scale=-1.0).then_inc(exp_ready, 1)

            def normalise(m, t):
                act.wait_ge(rstd_ready, m + 1)
                nc.scalar.activation(z[:, t, :], z[:, t, :], ACT.Identity, bias=shift[:, t:t + 1],
                                     scale=rstd[:, t:t + 1]).then_inc(norm_ready, 1)

            def square(m, t, place=exp_place):
                act.wait_ge(mean_ready, m + 1)
                nc.scalar.activation(place[t], z[:, t, :], ACT.Square,
                                     bias=minus_mean[:, t:t + 1],
                                     accum_out=sq_sum[:, t:t + 1]).then_inc(sq_ready, 1)

            def softmax_exp(b, g):
                lo, hi = GROUPS[g]
                act.wait_ge(softmax_step, SOFTMAX_STEPS * (2 * b + g) + 5)
                nc.scalar.activation(prob[:, lo:hi, :, :], expo[:, lo:hi, :, :], ACT.Exp).then_inc(prob_ready, 1)

            for k in range(K):
                act.wait_ge(W_loaded[k % T], 16 * (k // T + 1))
                nc.scalar.activation(W_high[:, k, :], z[:, k % T, :], ACT.Copy).then_inc(W_high_ready, 1)
                if k == 0:
                    split_x(0, 0)

            def batch(b, visit, q, first, last):
                for t in range(T):
                    n = T * b + t
                    if not first:
                        exp_z(n - T, t)
                    if t < T - 1 or not last:
                        split_x(n + 1, t + 1)
                    act.wait_ge(adjT_done, n + 1)
                    nc.scalar.activation(adjT[:, :, t * P:(t + 1) * P], adjT_ps[t % 2][:],
                                         ACT.Copy).then_inc(adjT_ready, 1)
                    if not first or t > 0:
                        act.wait_ge(adj_sq_ready, n)
                    nc.scalar.activation(adj_sq[:], adj_tile[:, t, :], ACT.Square,
                                         accum_out=adj_sq_sum[:, t:t + 1]).then_inc(adj_sq_ready, 1)
                    if not first and t > 0:
                        normalise(n - T - 1, t - 1)
                    for h in range(HALVES):
                        act.wait_ge(Wh_done, 2 * n + h + 1)
                        nc.scalar.activation(Wh_high[:, t, h * BANK:(h + 1) * BANK], Wh_ps[h][:],
                                             ACT.Copy).then_inc(Wh_high_ready, 1)
                        if h == 0 and not first and t < T - 1:
                            square(n - T, t)
                        if h == 0 and t == T - 1:
                            act.wait_ge(wide_summed, b + 1)
                            nc.scalar.activation(wide_count[:], adjT_ps[0][0:1, 0, 0:1], ACT.Copy)\
                                .then_inc(wide_count_ready, 1)
                            softmax_exp(b, 0)
                    if not first and t < T - 1:
                        if t > 0:
                            act.wait_ge(sq_ready, n - T)
                        below_zero(n - T + 1, t + 1)
                if not first:
                    square(T * b - 1, T - 1)
                    normalise(T * b - 1, T - 1)
                    act.wait_ge(sq_ready, T * b)
                if last:
                    below_zero(T * b, 0, exp_place_last)
                    exp_z(T * b, 0, exp_place_last)
                softmax_exp(b, 1)
                if not last:
                    below_zero(T * b, 0)

            over_batches(act, batch)
            m = T * (B - 1)
            below_zero(m + 1, 1, exp_place_last)
            exp_z(m + 1, 1, exp_place_last)
            for t in range(2, T):
                below_zero(m + t, t, exp_place_last)
                exp_z(m + t, t, exp_place_last)
                square(m + t - 2, t - 2, exp_place_last)
            normalise(m, 0)
            for t in range(T - 2, T):
                square(m + t, t, exp_place_last)
                normalise(m + t - 1, t - 1)
            normalise(m + T - 1, T - 1)

        @block.vector
        def _(dve):
            def split_x(n, t):
                for c in range(2):
                    chunks = slice(c * KB, (c + 1) * KB)
                    dve.wait_ge(xT_high_ready, 2 * n + c + 1)
                    nc.vector.tensor_tensor(xT_low[:, t % 2, chunks, :], xT_ps[c][:],
                                            xT_high[:, t % 2, chunks, :].bitcast(F32),
                                            ALU.subtract).then_inc(xT_low_ready, 1)

            def add_x(m, q, t, place=exp_place):
                dve.wait_ge(exp_ready, m + 1)
                nc.vector.scalar_tensor_tensor(place[t], place[t], -1.0, x_tile[:, q, t, :],
                                               ALU.add, ALU.add).then_inc(residual_ready, 1)

            def residual_sum(m, t, place=exp_place):
                dve.wait_ge(residual_ready, m + 1)
                nc.vector.scalar_tensor_tensor(z[:, t, :], z[:, t, :], 0.0, place[t],
                                               ALU.max, ALU.add,
                                               accum_out=row_sum[:, t:t + 1]).then_inc(y_ready, 1)
                dve.wait_ge(y_ready, m + 1)
                nc.vector.tensor_scalar(minus_mean[:, t:t + 1], row_sum[:, t:t + 1], -1.0 / D, None,
                                        ALU.mult).then_inc(mean_ready, 1)

            def split_Wh(n, t, h, start):
                cols = slice(h * BANK, (h + 1) * BANK)
                dve.wait_ge(Wh_high_ready, 2 * n + h + 1)
                nc.vector.tensor_tensor(Wh_low[:, t, cols], Wh_ps[h][:], Wh_high[:, t, cols].bitcast(F32),
                                        ALU.subtract).then_inc(Wh_low_ready, 1)
                if h == 0 and not start:
                    dve.wait_ge(head_sum_ready, n)
                nc.vector.tensor_tensor(Wh_a[:, cols], Wh_ps[h][:], a_sum[:, cols],
                                        ALU.mult).then_inc(Wh_a_ready, 1)

            def sum_heads(n, t):
                dve.wait_ge(Wh_a_ready, 2 * n + 2)
                nc.vector.tensor_reduce(head_sum[:, t, :], Wh_a[:].rearrange("p (h f) -> p h f", f=F),
                                        AX.X, ALU.add).then_inc(head_sum_ready, 1)

            def step(done, b, g, i):
                done.then_inc(softmax_step, 1)
                dve.wait_ge(softmax_step, SOFTMAX_STEPS * (2 * b + g) + i)

            def exponents(b, g, first):
                lo, hi = GROUPS[g]
                shape = [P, hi - lo, H]
                s, e, m = head_sum[:, lo:hi, :], e_act[:, lo:hi, :], row_max[:, lo:hi, :]
                dve.wait_ge(head_sum_ready, T * b + hi)
                if not first or g > 0:
                    dve.wait_ge(softmax_step, SOFTMAX_STEPS * (2 * b + g))
                dve.wait_ge(bound_ready, T * b + hi)
                step(nc.vector.scalar_tensor_tensor(e, s, ALPHA, s, ALU.mult, ALU.max), b, g, 1)
                step(nc.vector.tensor_tensor(m, e, bound[:, 0, lo:hi].unsqueeze(2).to_broadcast(shape), ALU.max),
                     b, g, 2)
                step(nc.vector.tensor_tensor(m, m, bound[:, 1, lo:hi].unsqueeze(2).to_broadcast(shape), ALU.min),
                     b, g, 3)
                nc.vector.tensor_scalar(expo[:, lo:hi, 1, :], m, -1.0, NEG_INF, ALU.mult, ALU.add)
                step(nc.vector.tensor_tensor(expo[:, lo:hi, 0, :], e, m, ALU.subtract), b, g, 4)
                nc.vector.tensor_scalar(expo[:, lo:hi, :, :], expo[:, lo:hi, :, :], 0.0, None,
                                        ALU.min).then_inc(softmax_step, 1)

            def scales(b, g, first):
                lo, hi = GROUPS[g]
                shape = [P, hi - lo, H]
                dve.wait_ge(prob_ready, 2 * b + g + 1)
                nc.vector.tensor_tensor(mass[:, lo:hi, 0, :], prob[:, lo:hi, 0, :],
                                        cnt[:, 0, lo:hi].unsqueeze(2).to_broadcast(shape), ALU.mult)
                step(nc.vector.tensor_tensor(mass[:, lo:hi, 1, :], prob[:, lo:hi, 1, :],
                                             cnt[:, 1, lo:hi].unsqueeze(2).to_broadcast(shape), ALU.mult),
                     b, g, 6)
                step(nc.vector.tensor_tensor(denom[:, lo:hi, :], mass[:, lo:hi, 0, :], mass[:, lo:hi, 1, :],
                                             ALU.add), b, g, 7)
                step(nc.vector.reciprocal(denom[:, lo:hi, :], denom[:, lo:hi, :]), b, g, 8)
                if not first:
                    dve.wait_ge(z_ready, 2 * T * b)
                step(nc.vector.tensor_tensor(att_scale[:, lo:hi, :], prob[:, lo:hi, 0, :], denom[:, lo:hi, :],
                                             ALU.mult), b, g, 9)

            def scale_rows(b, t, h, first):
                n = T * b + t
                dve.wait_ge(softmax_step, SOFTMAX_STEPS * (2 * b + (1 if t == T - 1 else 0) + 1))
                dve.wait_ge(hp_done, 2 * n + h + 1)
                if not first and h == 0:
                    dve.wait_ge(out_stored[t], 16 * b)
                nc.vector.tensor_tensor(
                    z[:, t, h * BANK:(h + 1) * BANK].rearrange("p (a f) -> p a f", f=F),
                    hp_ps[h][:].rearrange("p (a f) -> p a f", f=F),
                    att_scale[:, t, h * HB:(h + 1) * HB].unsqueeze(2).to_broadcast([P, HB, F]),
                    ALU.mult).then_inc(z_ready, 1)

            def adj_to_float(b, t):
                dve.wait_ge(adj_loaded[t], 16 * (b + 1))
                nc.vector.tensor_copy(adj_tile[:, t, :], adj_tile[:, t, :].bitcast(I32)).then_inc(adj_float, 1)

            for k in range(K):
                dve.wait_ge(W_high_ready, k + 1)
                nc.vector.tensor_tensor(W_low[:, k, :], z[:, k % T, :], W_high[:, k, :].bitcast(F32),
                                        ALU.subtract).then_inc(W_low_ready, 1)
                if k == 0:
                    split_x(0, 0)
                if k == K - 2:
                    adj_to_float(0, 0)
            split_x(1, 1)
            dve.wait_ge(a_loaded, 16)
            a_parts = elu_neg[:].rearrange("p q (h s f) -> p (q h) s f", s=2, f=F)
            nc.vector.tensor_tensor(a_sum[:].rearrange("p (h f) -> p h f", f=F), a_parts[:, :, 0, :],
                                    a_parts[:, :, 1, :], ALU.add).then_inc(a_sum_ready, 1)
            dve.wait_ge(a_sum_ready, 1)

            def count_neighbours(n, t, start):
                if not start:
                    dve.wait_ge(cnt_ready, n)
                dve.wait_ge(adj_float, n + 1)
                nc.vector.tensor_scalar(nonzero[:], adj_tile[:, t, :], 0.0, None, ALU.not_equal, ALU.add,
                                        accum_out=cnt[:, 0, t:t + 1]).then_inc(cnt_ready, 1)

            def split_adj(n, t):
                dve.wait_ge(adjT_ready, n + 1)
                nc.vector.tensor_tensor(adjT_low[:, :, t * P:(t + 1) * P], adjT_ps[t % 2][:],
                                        adjT[:, :, t * P:(t + 1) * P].bitcast(F32),
                                        ALU.subtract).then_inc(adjT_low_ready, 1)

            def batch(b, visit, q, first, last):
                for t in range(T):
                    n = T * b + t
                    if not first:
                        add_x(n - T, 1 - q, t)
                    if first and t == 0:
                        adj_to_float(b, 1)
                        split_Wh(n, t, 0, True)
                        split_Wh(n, t, 1, True)
                        split_adj(n, t)
                        count_neighbours(n, t, True)
                        sum_heads(n, t)
                        continue
                    if t < T - 1 or not last:
                        split_x(n + 1, t + 1)
                    if t < T - 1:
                        adj_to_float(b, t + 1)
                    elif not last:
                        adj_to_float(b + 1, 0)
                    count_neighbours(n, t, False)
                    split_adj(n, t)
                    if t == T - 1:
                        dve.wait_ge(adj_sq_ready, n + 1)
                        nc.vector.tensor_scalar(wide_row[:], adj_sq_sum[:], WIDE * WIDE, None, ALU.is_gt, ALU.add,
                                                accum_out=wide_rows[:]).then_inc(wide_ready, 1)
                    split_Wh(n, t, 0, False)
                    if t == T - 1:
                        exponents(b, 0, first)
                    if not first:
                        residual_sum(n - T, t)
                    if t == T - 1:
                        scales(b, 0, first)
                    split_Wh(n, t, 1, False)
                    if t < T - 1:
                        sum_heads(n, t)
                m = T * b
                scale_rows(b, 0, 0, first)
                scale_rows(b, 0, 1, first)
                sum_heads(m + T - 1, T - 1)
                scale_rows(b, 1, 0, first)
                exponents(b, 1, first)
                scale_rows(b, 1, 1, first)
                if last:
                    add_x(m, q, 0, exp_place_last)
                scale_rows(b, 2, 0, first)
                scales(b, 1, first)
                scale_rows(b, 2, 1, first)
                if last:
                    residual_sum(m, 0, exp_place_last)
                scale_rows(b, 3, 0, first)
                if last:
                    add_x(m + 1, q, 1, exp_place_last)
                scale_rows(b, 3, 1, first)
                if last:
                    residual_sum(m + 1, 1, exp_place_last)
                    for t in range(2, T):
                        add_x(m + t, q, t, exp_place_last)
                        residual_sum(m + t, t, exp_place_last)

            over_batches(dve, batch)

        @block.gpsimd
        def _(pool):
            pool.memset(ident[:], 0.0).then_inc(ident_ready, 1)
            pool.wait_ge(ident_ready, 1)
            pool.affine_select(out=ident[:], in_=ident[:], compare_op=ALU.not_equal, fill=1.0, base=0,
                               pattern=[[-1, P]], channel_multiplier=1).then_inc(ident_ready, 1)
            for const, value in ((half_power, -0.5), (nodes, float(N)), (inverse_D, 1.0 / D), (eps, EPS),
                                 (neg_inf, NEG_INF), (ones, 1.0)):
                pool.memset(const[:], value).then_inc(const_ready, 1)
            pool.wait_ge(const_ready, 6)

            def row_bounds(n, t, start):
                pool.wait_ge(cnt_ready, n + 1)
                if not start:
                    pool.wait_ge(bound_ready, n)
                c = cnt[:, 0, t:t + 1]
                pool.tensor_tensor(cnt[:, 1, t:t + 1], nodes[:], c, ALU.subtract)
                pool.tensor_scalar(bound[:, 0, t:t + 1], c, float(N), -BIG, ALU.is_ge, ALU.mult)\
                    .then_inc(bound_raw, 1)
                pool.tensor_scalar(bound[:, 1, t:t + 1], c, 0.0, BIG, ALU.is_gt, ALU.mult).then_inc(bound_raw, 1)
                pool.wait_ge(bound_raw, 2 * n + 2)
                pool.tensor_tensor(bound[:, :, t:t + 1], bound[:, :, t:t + 1], neg_inf[:].unsqueeze(2), ALU.add)\
                    .then_inc(bound_ready, 1)

            def inverse_std(m, t):
                pool.wait_ge(sq_ready, m + 1)
                pool.tensor_tensor(var[:, t:t + 1], sq_sum[:, t:t + 1], inverse_D[:], ALU.mult)\
                    .then_inc(var_step, 1)
                pool.wait_ge(var_step, 2 * m + 1)
                pool.tensor_tensor(var_eps[:, t:t + 1], var[:, t:t + 1], eps[:], ALU.add).then_inc(var_step, 1)
                pool.wait_ge(var_step, 2 * m + 2)
                pool.tensor_tensor(rstd[:, t:t + 1], var_eps[:, t:t + 1], half_power[:],
                                   ALU.pow).then_inc(power_ready, 1)
                pool.wait_ge(power_ready, m + 1)
                pool.tensor_tensor(shift[:, t:t + 1], minus_mean[:, t:t + 1], rstd[:, t:t + 1],
                                   ALU.mult).then_inc(rstd_ready, 1)


            def batch(b, visit, q, first, last):
                for t in range(T):
                    n = T * b + t
                    row_bounds(n, t, first and t == 0)
                    if not first:
                        inverse_std(n - T, t)

            over_batches(pool, batch)
            for t in range(T):
                inverse_std(T * (B - 1) + t, t)


def kernel(x, adj, L0_gnn_W, L0_gnn_a):
    import numpy as np
    import concourse.bacc as bacc
    from concourse.bass_utils import run_bass_kernel_spmd

    nc = bacc.Bacc("TRN2", target_bir_lowering=False, num_devices=1)
    arrays, args = {}, []
    for name, value in (("x", x), ("adj", adj), ("W", L0_gnn_W), ("a", L0_gnn_a)):
        arrays[f"in_{name}"] = np.ascontiguousarray(value)
        args.append(nc.dram_tensor(f"in_{name}", arrays[f"in_{name}"].shape,
                                   mybir.dt.from_np(arrays[f"in_{name}"].dtype), kind="ExternalInput").ap())
    out = nc.dram_tensor("out", arrays["in_x"].shape, F32, kind="ExternalOutput").ap()
    gat_layer(nc, *args, out)
    result = run_bass_kernel_spmd(nc, [arrays], core_ids=[0])
    return result.results[0]["out"]
```
